# Optimizing a Trainium2 kernel written in Bass

```python
import numpy as np
import jax
import jax.numpy as jnp

def _softmax(x, axis=-1):
    return jax.nn.softmax(x, axis=axis)

def _gelu(x):
    return jax.nn.gelu(x, approximate=True)

def _silu(x):
    return jax.nn.silu(x)

def _sigmoid(x):
    return jax.nn.sigmoid(x)

def _layernorm(x, axis=-1, eps=1e-05):
    m = jnp.mean(x, axis=axis, keepdims=True)
    v = jnp.var(x, axis=axis, keepdims=True)
    return (x - m) / jnp.sqrt(v + eps)

def _scatter_add(tgt, idx, src, axis=0):
    return tgt.at[idx].add(src)

def _segment_sum(src, seg, n):
    return jax.ops.segment_sum(src, seg, n)
kernel_name = 'mk_rec_standalone_d1_rec_r8_388207'

def setup_inputs(seed: int=0):
    np.random.seed(seed)
    _w = jnp.asarray

    def _rec_inputs():
        import jax
        import jax.numpy as jnp
        _rk = jax.random.key(seed)
        r_dense_features = 0.00021031 + 1.00007 * jax.random.normal(jax.random.fold_in(_rk, 1), (2048, 64, 128), jnp.float32)
        return r_dense_features
    r_dense_features = _rec_inputs()

    def _L0_rec_setup():
        import jax, jax.numpy as jnp
        import numpy as np
        NUM_FEATURES = 64
        _IU, _JU = np.triu_indices(NUM_FEATURES, k=1)
        _IU = jnp.asarray(_IU)
        _JU = jnp.asarray(_JU)
        key = jax.random.key(seed)
        dense_features = jax.random.normal(key, (512, NUM_FEATURES, 128), dtype=jnp.float32)
        return {'dense_features': dense_features}
    _L0_rec_all = _L0_rec_setup()
    _L0_rec_in = {k: v for k, v in _L0_rec_all.items() if k in ()}
    del _L0_rec_all
    return {'r_dense_features': r_dense_features}

def reference(r_dense_features):
    import jax
    import jax.numpy as jnp

    def _L0_rec_ref(dense_features):
        import jax, jax.numpy as jnp
        import numpy as np
        NUM_FEATURES = 64
        _IU, _JU = np.triu_indices(NUM_FEATURES, k=1)
        _IU = jnp.asarray(_IU)
        _JU = jnp.asarray(_JU)
        gram = jnp.einsum('bfd,bgd->bfg', dense_features, dense_features)
        return gram[:, _IU, _JU]
    y = _L0_rec_ref(r_dense_features)
    return y

_drawn_inputs = setup_inputs


def setup_inputs(seed=0):
    import zlib

    import numpy as np

    out = dict(_drawn_inputs(seed))
    spreads = {}
    factors = {}
    for name, (base, spread) in spreads.items():
        noise = np.random.default_rng([zlib.crc32(name.encode()), seed]).standard_normal(out[name].shape)
        drawn = base * np.exp(spread * noise) if base else spread * noise
        out[name] = jnp.asarray(drawn.astype(out[name].dtype))
    for name, factor in factors.items():
        out[name] = (out[name] * factor).astype(out[name].dtype)
    return out
```

```python
import concourse.bass as bass
from concourse import mybir
from contextlib import ExitStack


def build_gram_triangle(nc, x, out):
    fp32 = mybir.dt.float32
    ACT = mybir.ActivationFunctionType
    ALU = mybir.AluOpType

    P = 128
    B, F, D = x.shape
    TRI = out.shape[1]
    assert 2 * F == P and D == P and TRI == F * (F - 1) // 2
    ROWS_PER_PART = 16
    BLOCK_ROWS = P * ROWS_PER_PART
    BLOCKS = B * F // BLOCK_ROWS
    BLOCK_PAIRS = BLOCK_ROWS // P
    GROUP_PAIRS = P
    GROUP_BLOCKS = GROUP_PAIRS // BLOCK_PAIRS
    GROUPS = BLOCKS // GROUP_BLOCKS
    BANK = 512
    PER_BANK = BANK // P
    QUARTERS = ROWS_PER_PART // PER_BANK
    assert QUARTERS * PER_BANK == BLOCK_PAIRS
    CHUNK = BANK // 2
    X_SLOTS, FLIP_SLOTS = 4, 2
    FLIP_BANKS, GRAM_BANKS, TRI_BANKS = 2, 4, 2
    assert GROUPS % 2 == 0 and GROUP_BLOCKS % X_SLOTS == 0

    row_start = [c * (F - 1) - c * (c - 1) // 2 for c in range(F)]
    chunks = [[0]]
    for c in range(1, F - 1):
        if row_start[c] + F - row_start[chunks[-1][0]] > CHUNK:
            chunks.append([])
        chunks[-1].append(c)
    CHUNKS = len(chunks)
    chunk_start = [row_start[rows[0]] for rows in chunks] + [TRI]
    beside = {}
    for v in range(CHUNKS):
        u = v * GROUP_BLOCKS // CHUNKS
        beside[u, 3 if (u, 1) in beside else 1] = v
    assert len(beside) == CHUNKS
    HALVES = 2
    half_chunks = [0, (CHUNKS + 1) // 2, CHUNKS]
    half_start = [chunk_start[v] for v in half_chunks]
    half_block = [(half_chunks[h + 1] - 1) * GROUP_BLOCKS // CHUNKS for h in range(HALVES)]

    x_blocks = x.rearrange("(k b) f d -> k (b f) d", k=BLOCKS).rearrange(
        "k (p j) d -> k p (j d)", j=ROWS_PER_PART)
    out_groups = out.rearrange("(g p two) t -> g p two t", g=GROUPS, two=2)

    ctx = ExitStack()
    with ctx:
        def sb(name, shape):
            return ctx.enter_context(nc.sbuf_tensor(name, shape, fp32))

        def sem(name):
            return ctx.enter_context(nc.semaphore(name))

        x_rows = sb("x_rows", [P, X_SLOTS, ROWS_PER_PART * D])
        x_flipped = sb("x_flipped", [P, FLIP_SLOTS, BLOCK_ROWS])
        grams = sb("grams", [P, 2, F, GROUP_PAIRS])
        triangles = sb("triangles", [P, 2, 2, TRI])
        ident = sb("ident", [P, P])
        turns = sb("turns", [P, 2, 2 * F])
        flip_ps = [ctx.enter_context(nc.psum_tensor(f"flip_ps{i}", [P, BANK], fp32)) for i in range(FLIP_BANKS)]
        gram_ps = [ctx.enter_context(nc.psum_tensor(f"gram_ps{i}", [P, BANK], fp32)) for i in range(GRAM_BANKS)]
        tri_ps = [ctx.enter_context(nc.psum_tensor(f"tri_ps{i}", [P, BANK], fp32)) for i in range(TRI_BANKS)]

        zeroed = sem("zeroed")
        ident_ready = sem("ident_ready")
        x_loaded = [sem(f"x_loaded{i}") for i in range(X_SLOTS)]
        flip_in_psum = sem("flip_in_psum")
        flip_in_sbuf = sem("flip_in_sbuf")
        gram_in_psum = sem("gram_in_psum")
        gram_in_sbuf = sem("gram_in_sbuf")
        tri_in_psum = sem("tri_in_psum")
        tri_in_sbuf = sem("tri_in_sbuf")
        stored = [sem(f"stored{h}") for h in range(HALVES)]
        block = ctx.enter_context(nc.Block())

        def over_groups(engine, body):
            body(0, 0)
            with engine.Fori(0, (GROUPS - 2) // 2) as i:
                body(i * 2 + 1, 1)
                body(i * 2 + 2, 0)
            body(GROUPS - 1, 1)

        def first(g):
            return isinstance(g, int) and g == 0

        def last(g):
            return isinstance(g, int) and g == GROUPS - 1

        @block.gpsimd
        def _(pool):
            pool.memset(ident[:, :], 0.0).then_inc(zeroed, 1)
            pool.memset(turns[:, :, :], 0.0).then_inc(zeroed, 1)
            pool.wait_ge(zeroed, 2)
            pool.affine_select(out=ident[:, :], in_=ident[:, :], compare_op=ALU.not_equal, fill=1.0,
                               base=0, pattern=[[-1, P]], channel_multiplier=1).then_inc(ident_ready, 1)
            twice = turns[:, :, :].rearrange("p two (n r) -> p two n r", n=2)
            pool.affine_select(out=twice, in_=twice, compare_op=ALU.not_equal, fill=1.0,
                               base=0, pattern=[[-F, 2], [0, 2], [-1, F]], channel_multiplier=1).then_inc(ident_ready, 1)

        @block.sync
        def _(sp):
            for k in range(X_SLOTS):
                sp.dma_start(x_rows[:, k, :], x_blocks[k]).then_inc(x_loaded[k], 16)

            def store(g, parity, h):
                sp.wait_ge(tri_in_sbuf, g * CHUNKS + half_chunks[h + 1])
                a, b = half_start[h], half_start[h + 1]
                sp.dma_start(out_groups[g][:, :, a:b], triangles[:, parity, :, a:b]).then_inc(stored[h], 16)

            def body(g, parity):
                for u in range(GROUP_BLOCKS):
                    if not (last(g) and u + X_SLOTS >= GROUP_BLOCKS):
                        sp.wait_ge(flip_in_psum, (g * GROUP_BLOCKS + u + 1) * QUARTERS)
                        sp.dma_start(x_rows[:, u % X_SLOTS, :], x_blocks[g * GROUP_BLOCKS + (u + X_SLOTS)])\
                          .then_inc(x_loaded[u % X_SLOTS], 16)
                    if not first(g) and u in half_block:
                        store(g - 1, 1 - parity, half_block.index(u))

            over_groups(sp, body)
            for h in range(HALVES):
                store(GROUPS - 1, 1, h)
            for h in range(HALVES):
                sp.wait_ge(stored[h], 16 * GROUPS)

        @block.tensor
        def _(pe):
            def flip(g, u, q):
                if q == 0:
                    pe.wait_ge(x_loaded[u % X_SLOTS],
                               (g * (GROUP_BLOCKS // X_SLOTS) + (u // X_SLOTS + 1)) * 16)
                if not (first(g) and u * QUARTERS + q < FLIP_BANKS):
                    pe.wait_ge(flip_in_sbuf, g * GROUP_BLOCKS * QUARTERS + (u * QUARTERS + q + 1 - FLIP_BANKS))
                for n in range(PER_BANK):
                    j = q * PER_BANK + n
                    t = pe.transpose(flip_ps[q % FLIP_BANKS][:, n * P:(n + 1) * P],
                                     x_rows[:, u % X_SLOTS, j * D:(j + 1) * D], ident[:, :])
                t.then_inc(flip_in_psum, 1)

            def gram(g, u, q):
                if q == 0:
                    pe.wait_ge(flip_in_sbuf, (g * GROUP_BLOCKS + (u + 1)) * QUARTERS)
                if not (first(g) and u * QUARTERS + q < GRAM_BANKS):
                    pe.wait_ge(gram_in_sbuf, g * GROUP_BLOCKS * QUARTERS + (u * QUARTERS + q + 1 - GRAM_BANKS))
                for n in range(PER_BANK):
                    t = (q * PER_BANK + n) * P
                    pair = x_flipped[:, u % FLIP_SLOTS, t:t + P]
                    m = pe.matmul(gram_ps[q % GRAM_BANKS][:, n * P:(n + 1) * P], pair, pair, start=True, stop=True)
                m.then_inc(gram_in_psum, 1)

            def triangle(g, parity, v):
                if v == 0:
                    pe.wait_ge(gram_in_sbuf, (g + 1) * (GROUP_BLOCKS * QUARTERS))
                if last(g):
                    pe.wait_ge(tri_in_sbuf, g * CHUNKS + (v + 1 - TRI_BANKS))
                to = tri_ps[v % TRI_BANKS][:, :].rearrange("p (two t) -> p two t", two=2)
                for c in chunks[v]:
                    at = row_start[c] - chunk_start[v]
                    t = pe.transpose(to[:, :, at:at + F], grams[:, parity, c, :], turns[:, :, c + 1:c + 1 + F])
                t.then_inc(tri_in_psum, 1)

            def body(g, parity):
                for u in range(GROUP_BLOCKS):
                    for q in range(QUARTERS):
                        if not (last(g) and u == GROUP_BLOCKS - 1):
                            flip(g, u + 1, q)
                        gram(g, u, q)
                        if (u, q) in beside and not first(g):
                            triangle(g - 1, 1 - parity, beside[u, q])

            pe.wait_ge(ident_ready, 2)
            for q in range(QUARTERS):
                flip(0, 0, q)
            over_groups(pe, body)
            for v in range(CHUNKS):
                triangle(GROUPS - 1, 1, v)

        @block.scalar
        def _(act):
            def flip_out(g, u, q):
                act.wait_ge(flip_in_psum, g * GROUP_BLOCKS * QUARTERS + (u * QUARTERS + q + 1))
                rows = x_flipped[:, u % FLIP_SLOTS, :].rearrange("d (p j) -> d j p", j=ROWS_PER_PART)
                act.activation(rows[:, q * PER_BANK:(q + 1) * PER_BANK, :],
                               flip_ps[q % FLIP_BANKS][:, :].rearrange("d (j p) -> d j p", p=P), ACT.Copy)\
                   .then_inc(flip_in_sbuf, 1)

            def triangle_out(g, parity, v):
                if parity == 1 and v in half_chunks:
                    act.wait_ge(stored[half_chunks.index(v)], g * 16)
                act.wait_ge(tri_in_psum, g * CHUNKS + (v + 1))
                a, b = chunk_start[v], chunk_start[v + 1]
                act.activation(triangles[:, parity, :, a:b],
                               tri_ps[v % TRI_BANKS][:, :].rearrange("p (two t) -> p two t", two=2)[:, :, 0:b - a],
                               ACT.Copy).then_inc(tri_in_sbuf, 1)

            def body(g, parity):
                for u in range(GROUP_BLOCKS):
                    for q in range(QUARTERS):
                        if not (last(g) and u == GROUP_BLOCKS - 1):
                            flip_out(g, u + 1, q)
                        if (u, q) in beside and not first(g):
                            triangle_out(g - 1, 1 - parity, beside[u, q])

            for q in range(QUARTERS):
                flip_out(0, 0, q)
            over_groups(act, body)
            for v in range(CHUNKS):
                triangle_out(GROUPS - 1, 1, v)

        @block.vector
        def _(dve):
            def body(g, parity):
                for u in range(GROUP_BLOCKS):
                    for q in range(QUARTERS):
                        dve.wait_ge(gram_in_psum, g * GROUP_BLOCKS * QUARTERS + (u * QUARTERS + q + 1))
                        both = gram_ps[q % GRAM_BANKS][:, :].rearrange("r (n c) -> r n c", c=P)
                        t = u * BLOCK_PAIRS + q * PER_BANK
                        to = grams[:, parity, 0:F - 1, t:t + PER_BANK].rearrange("r c n -> r n c")
                        dve.tensor_copy(to[0:F], both[0:F, :, 0:F - 1])
                        dve.tensor_copy(to[F:P], both[F:P, :, F:P - 1]).then_inc(gram_in_sbuf, 1)

            over_groups(dve, body)


def kernel(r_dense_features):
    import numpy as np
    import concourse.bacc as bacc
    from concourse.bass_utils import run_bass_kernel_spmd

    x = np.ascontiguousarray(r_dense_features)
    b, f, _ = x.shape
    nc = bacc.Bacc("TRN2", target_bir_lowering=False, num_devices=1)
    x_dram = nc.dram_tensor("x_dram", x.shape, mybir.dt.float32, kind="ExternalInput").ap()
    out_dram = nc.dram_tensor("out_dram", (b, f * (f - 1) // 2), mybir.dt.float32, kind="ExternalOutput").ap()
    build_gram_triangle(nc, x_dram, out_dram)
    r = run_bass_kernel_spmd(nc, [{"x_dram": x}], core_ids=[0])
    return r.results[0]["out_dram"]
```

```python
import concourse.bass as bass
from concourse import mybir
from contextlib import ExitStack


def build_gram_triangle(nc, x, out):
    fp32 = mybir.dt.float32
    ACT = mybir.ActivationFunctionType
    ALU = mybir.AluOpType

    P = 128
    B, F, D = x.shape
    TRI = out.shape[1]
    assert 2 * F == P and D == P and TRI == F * (F - 1) // 2
    ROWS_PER_PART = 16
    BLOCK_ROWS = P * ROWS_PER_PART
    BLOCKS = B * F // BLOCK_ROWS
    BLOCK_PAIRS = BLOCK_ROWS // P
    QUAD = 32
    QUADS = P // QUAD
    GROUP_PAIRS = P
    GROUP_BLOCKS = GROUP_PAIRS // BLOCK_PAIRS
    GROUPS = BLOCKS // GROUP_BLOCKS
    BANK = 512
    PER_BANK = BANK // P
    QUARTERS = ROWS_PER_PART // PER_BANK
    assert QUARTERS * PER_BANK == BLOCK_PAIRS
    QUAD_BLOCKS = GROUP_BLOCKS // QUADS
    assert F == 2 * QUAD and QUAD_BLOCKS * BLOCK_PAIRS == QUAD
    X_SLOTS, FLIP_SLOTS = 4, 2
    FLIP_BANKS, GRAM_BANKS = 4, 4
    assert QUARTERS % GRAM_BANKS == 0 and QUARTERS % FLIP_BANKS == 0
    assert GROUPS % 2 == 0 and GROUP_BLOCKS % X_SLOTS == 0

    row_start = [c * (F - 1) - c * (c - 1) // 2 for c in range(F)]
    STEP = 8
    low = [[("lower", c) for c in range(a, min(a + STEP, QUAD - 1))] for a in range(0, QUAD, STEP)]
    up = [[("upper", c) for c in range(a, a + STEP)] for a in range(0, QUAD, STEP)]
    chunks = [[("apart", a, min(a + QUAD // 2, F - 1))] for a in (QUAD, QUAD + QUAD // 2)]
    APART_CHUNKS = len(chunks)
    chunks.append(low[0])
    for n in range(1, len(low)):
        chunks += [low[n], up[n - 1]]
    chunks.append(up[-1])
    CHUNKS = len(chunks)
    TOLD_CHUNKS = CHUNKS - 1
    FIRST_QUARTER = 4
    beside = {FIRST_QUARTER + 2 * v: v for v in range(CHUNKS)}
    assert max(beside) + 1 + GRAM_BANKS < GROUP_BLOCKS * QUARTERS
    LOT = 7
    lots = [range(a, min(a + LOT, F - 1)) for a in range(QUAD, F - 1, LOT)]
    LOTS = len(lots)
    lot_beside = {FIRST_QUARTER + 2 * APART_CHUNKS + 1 + 2 * n: n for n in range(LOTS)}
    PARTS = 2
    part_chunks = [chunks.index(up[1]) + 1, CHUNKS]
    part_start = [0, row_start[2 * STEP], TRI]
    part_block = [(FIRST_QUARTER + 2 * (n - 1)) // QUARTERS for n in part_chunks]

    x_blocks = x.rearrange("(k b) f d -> k (b f) d", k=BLOCKS).rearrange(
        "k (p j) d -> k p (j d)", j=ROWS_PER_PART)
    out_groups = out.rearrange("(g p two) t -> g p two t", g=GROUPS, two=2)

    ctx = ExitStack()
    with ctx:
        def sb(name, shape):
            return ctx.enter_context(nc.sbuf_tensor(name, shape, fp32))

        def sem(name):
            return ctx.enter_context(nc.semaphore(name))

        x_rows = sb("x_rows", [P, X_SLOTS, ROWS_PER_PART * D])
        x_flipped = sb("x_flipped", [P, FLIP_SLOTS, BLOCK_ROWS])
        lower = sb("lower", [P, 2, QUAD - 1, 2, QUAD])
        upper = sb("upper", [P, 2, F - 1, 2, QUAD])
        triangles = [sb(f"triangles{i}", [P, 2, 1 + TRI]) for i in range(2)]
        apart = sb("apart", [P, 2, F - 1 - QUAD, 2, QUAD])
        ident = sb("ident", [P, P])
        flip_ps = [ctx.enter_context(nc.psum_tensor(f"flip_ps{i}", [P, BANK], fp32)) for i in range(FLIP_BANKS)]
        gram_ps = [ctx.enter_context(nc.psum_tensor(f"gram_ps{i}", [P, BANK], fp32)) for i in range(GRAM_BANKS)]
        zeroed = sem("zeroed")
        ident_ready = sem("ident_ready")
        x_loaded = [sem(f"x_loaded{i}") for i in range(X_SLOTS)]
        flip_in_psum = sem("flip_in_psum")
        flip_in_sbuf = sem("flip_in_sbuf")
        gram_in_psum = sem("gram_in_psum")
        even_in_sbuf = sem("even_in_sbuf")
        odd_in_sbuf = sem("odd_in_sbuf")
        tri_in_sbuf = sem("tri_in_sbuf")
        rest_written = sem("rest_written")
        stored = [sem(f"stored{h}") for h in range(PARTS)]
        block = ctx.enter_context(nc.Block())

        def over_groups(engine, body):
            body(0, 0)
            with engine.Fori(0, (GROUPS - 2) // 2) as i:
                body(i * 2 + 1, 1)
                body(i * 2 + 2, 0)
            body(GROUPS - 1, 1)

        def gram_parts(parity, u, q):
            products = gram_ps[q % GRAM_BANKS][:, :].rearrange("r (n c) -> r n c", c=P)
            to = slice(u // QUAD_BLOCKS * QUAD, (u // QUAD_BLOCKS + 1) * QUAD)
            pair = u % QUAD_BLOCKS * BLOCK_PAIRS + q * PER_BANK
            for two in range(2):
                for half, rows in enumerate((lower, upper)):
                    r, columns = two * F + half * QUAD, rows.shape[2]
                    yield (rows[to, parity, :, two, pair:pair + PER_BANK].rearrange("r c n -> r n c"),
                           products[r:r + QUAD, :, two * F:two * F + columns])

        def first(g):
            return isinstance(g, int) and g == 0

        def last(g):
            return isinstance(g, int) and g == GROUPS - 1

        @block.gpsimd
        def _(pool):
            pool.memset(ident[:, :], 0.0).then_inc(zeroed, 1)
            pool.wait_ge(zeroed, 1)
            pool.affine_select(out=ident[:, :], in_=ident[:, :], compare_op=ALU.not_equal, fill=1.0,
                               base=0, pattern=[[-1, P]], channel_multiplier=1).then_inc(ident_ready, 1)

        @block.sync
        def _(sp):
            for k in range(X_SLOTS):
                sp.dma_start(x_rows[:, k, :], x_blocks[k]).then_inc(x_loaded[k], 16)

            def store(g, parity, h):
                if h == 0:
                    sp.wait_ge(tri_in_sbuf, g * TOLD_CHUNKS + part_chunks[0])
                else:
                    sp.wait_ge(rest_written, (g + 1) * (1 + LOTS))
                a, b = part_start[h], part_start[h + 1]
                sp.dma_start(out_groups[g][:, :, a:b], triangles[parity][:, :, 1 + a:1 + b]).then_inc(stored[h], 16)

            def body(g, parity):
                for u in range(GROUP_BLOCKS):
                    if not (last(g) and u + X_SLOTS >= GROUP_BLOCKS):
                        sp.wait_ge(flip_in_psum, (g * GROUP_BLOCKS + u + 1) * QUARTERS)
                        sp.dma_start(x_rows[:, u % X_SLOTS, :], x_blocks[g * GROUP_BLOCKS + (u + X_SLOTS)])\
                          .then_inc(x_loaded[u % X_SLOTS], 16)
                    if not first(g) and u in part_block:
                        store(g - 1, 1 - parity, part_block.index(u))

            over_groups(sp, body)
            for h in range(PARTS):
                store(GROUPS - 1, 1, h)
            for h in range(PARTS):
                sp.wait_ge(stored[h], 16 * GROUPS)

        @block.tensor
        def _(pe):
            def flip(g, u, q):
                if q == 0:
                    pe.wait_ge(x_loaded[u % X_SLOTS],
                               (g * (GROUP_BLOCKS // X_SLOTS) + (u // X_SLOTS + 1)) * 16)
                if not (first(g) and u * QUARTERS + q < FLIP_BANKS):
                    pe.wait_ge(flip_in_sbuf, g * GROUP_BLOCKS * QUARTERS + (u * QUARTERS + q + 1 - FLIP_BANKS))
                for n in range(PER_BANK):
                    j = q * PER_BANK + n
                    t = pe.transpose(flip_ps[q % FLIP_BANKS][:, n * P:(n + 1) * P],
                                     x_rows[:, u % X_SLOTS, j * D:(j + 1) * D], ident[:, :])
                t.then_inc(flip_in_psum, 1)

            def gram(g, u, q):
                if q == 0:
                    pe.wait_ge(flip_in_sbuf, (g * GROUP_BLOCKS + (u + 1)) * QUARTERS)
                if not (first(g) and u * QUARTERS + q < GRAM_BANKS):
                    pe.wait_ge(odd_in_sbuf if q % 2 else even_in_sbuf,
                               g * (GROUP_BLOCKS * QUARTERS // 2) + (u * QUARTERS + q + 2 - GRAM_BANKS) // 2)
                for n in range(PER_BANK):
                    t = (q * PER_BANK + n) * P
                    pair = x_flipped[:, u % FLIP_SLOTS, t:t + P]
                    m = pe.matmul(gram_ps[q % GRAM_BANKS][:, n * P:(n + 1) * P], pair, pair, start=True, stop=True)
                m.then_inc(gram_in_psum, 1)

            def body(g, parity):
                for u in range(GROUP_BLOCKS):
                    for q in range(QUARTERS):
                        if not (last(g) and u == GROUP_BLOCKS - 1):
                            flip(g, u + 1, q)
                        gram(g, u, q)

            pe.wait_ge(ident_ready, 1)
            for q in range(QUARTERS):
                flip(0, 0, q)
            over_groups(pe, body)

        @block.scalar
        def _(act):
            def flip_out(g, u, q):
                act.wait_ge(flip_in_psum, g * GROUP_BLOCKS * QUARTERS + (u * QUARTERS + q + 1))
                rows = x_flipped[:, u % FLIP_SLOTS, :].rearrange("d (p j) -> d j p", j=ROWS_PER_PART)
                act.activation(rows[:, q * PER_BANK:(q + 1) * PER_BANK, :],
                               flip_ps[q % FLIP_BANKS][:, :].rearrange("d (j p) -> d j p", p=P), ACT.Copy)\
                   .then_inc(flip_in_sbuf, 1)

            def copy_apart(g, parity, n):
                if n == 0:
                    act.wait_ge(tri_in_sbuf, g * TOLD_CHUNKS + APART_CHUNKS)
                for c in lots[n]:
                    a = act.activation(triangles[parity][:, :, 1 + row_start[c]:1 + row_start[c + 1]],
                                       apart[:, parity, c - QUAD, :, c + 1 - QUAD:QUAD], ACT.Copy)
                a.then_inc(rest_written, 1)

            def body(g, parity):
                for u in range(GROUP_BLOCKS):
                    for q in range(QUARTERS):
                        if not (last(g) and u == GROUP_BLOCKS - 1):
                            flip_out(g, u + 1, q)
                        if q % 2 == 0:
                            act.wait_ge(gram_in_psum, g * GROUP_BLOCKS * QUARTERS + (u * QUARTERS + q + 1))
                            for to, products in gram_parts(parity, u, q):
                                a = act.activation(to, products, ACT.Copy)
                            a.then_inc(even_in_sbuf, 1)
                        if u * QUARTERS + q in lot_beside and not first(g):
                            copy_apart(g - 1, 1 - parity, lot_beside[u * QUARTERS + q])

            for q in range(QUARTERS):
                flip_out(0, 0, q)
            over_groups(act, body)
            for n in range(LOTS):
                copy_apart(GROUPS - 1, 1, n)

        @block.vector
        def _(dve):
            def triangle(g, parity, v):
                if v == 0:
                    dve.wait_ge(even_in_sbuf, (g + 1) * (GROUP_BLOCKS * QUARTERS // 2))
                    dve.wait_ge(odd_in_sbuf, (g + 1) * (GROUP_BLOCKS * QUARTERS // 2))
                    if parity == 1:
                        for h in range(PARTS):
                            dve.wait_ge(stored[h], g * 16)
                else:
                    dve.wait_ge(tri_in_sbuf, g * TOLD_CHUNKS + v)
                for kind, c, *end in chunks[v]:
                    if kind == "apart":
                        t = dve.transpose(apart[:, parity, c - QUAD:end[0] - QUAD], upper[:, parity, c:end[0]])
                        continue
                    at = 1 + row_start[c] - (c + 1) + (QUAD if kind == "upper" else 0)
                    t = dve.transpose(triangles[parity][:, :, at:at + QUAD],
                                      (upper if kind == "upper" else lower)[:, parity, c])
                t.then_inc(tri_in_sbuf if v < TOLD_CHUNKS else rest_written, 1)

            def body(g, parity):
                for u in range(GROUP_BLOCKS):
                    for q in range(QUARTERS):
                        if q % 2:
                            dve.wait_ge(gram_in_psum, g * GROUP_BLOCKS * QUARTERS + (u * QUARTERS + q + 1))
                            for to, products in gram_parts(parity, u, q):
                                t = dve.tensor_copy(to, products)
                            t.then_inc(odd_in_sbuf, 1)
                        if u * QUARTERS + q in beside and not first(g):
                            triangle(g - 1, 1 - parity, beside[u * QUARTERS + q])

            over_groups(dve, body)
            for v in range(CHUNKS):
                triangle(GROUPS - 1, 1, v)


def kernel(r_dense_features):
    import numpy as np
    import concourse.bacc as bacc
    from concourse.bass_utils import run_bass_kernel_spmd

    x = np.ascontiguousarray(r_dense_features)
    b, f, _ = x.shape
    nc = bacc.Bacc("TRN2", target_bir_lowering=False, num_devices=1)
    x_dram = nc.dram_tensor("x_dram", x.shape, mybir.dt.float32, kind="ExternalInput").ap()
    out_dram = nc.dram_tensor("out_dram", (b, f * (f - 1) // 2), mybir.dt.float32, kind="ExternalOutput").ap()
    build_gram_triangle(nc, x_dram, out_dram)
    r = run_bass_kernel_spmd(nc, [{"x_dram": x}], core_ids=[0])
    return r.results[0]["out_dram"]
```

```python
import concourse.bass as bass
from concourse import mybir
from contextlib import ExitStack


def build_gram_triangle(nc, x, out):
    fp32 = mybir.dt.float32
    ACT = mybir.ActivationFunctionType
    ALU = mybir.AluOpType

    P = 128
    B, F, D = x.shape
    TRI = out.shape[1]
    assert 2 * F == P and D == P and TRI == F * (F - 1) // 2
    ROWS_PER_PART = 16
    BLOCK_ROWS = P * ROWS_PER_PART
    BLOCKS = B * F // BLOCK_ROWS
    BLOCK_PAIRS = BLOCK_ROWS // P
    QUAD = 32
    QUADS = P // QUAD
    GROUP_PAIRS = P
    GROUP_BLOCKS = GROUP_PAIRS // BLOCK_PAIRS
    GROUPS = BLOCKS // GROUP_BLOCKS
    BANK = 512
    PER_BANK = BANK // P
    QUARTERS = ROWS_PER_PART // PER_BANK
    assert QUARTERS * PER_BANK == BLOCK_PAIRS
    QUAD_BLOCKS = GROUP_BLOCKS // QUADS
    assert F == 2 * QUAD and QUAD_BLOCKS * BLOCK_PAIRS == QUAD
    X_SLOTS, FLIP_SLOTS = 4, 2
    FLIP_BANKS, GRAM_BANKS = 4, 4
    PIECED = 2
    assert QUARTERS % GRAM_BANKS == 0 and QUARTERS % FLIP_BANKS == 0
    assert GROUPS % 2 == 0 and GROUP_BLOCKS % X_SLOTS == 0

    row_start = [c * (F - 1) - c * (c - 1) // 2 for c in range(F)]
    STEP = 8

    def cut(a, b, step):
        return [range(n, min(n + step, b)) for n in range(a, b, step)]

    lower_apart, upper_apart = cut(0, QUAD - 1, QUAD // 2), cut(QUAD, F - 1, QUAD // 2)
    squares, lower_lots, upper_lots = cut(0, QUAD, STEP), cut(0, QUAD - 1, STEP), cut(QUAD, F - 1, 6)
    chunks = ([("apart", c) for c in upper_apart + lower_apart] + [("squares", c) for c in squares]
              + [("lot", c) for c in lower_lots])
    CHUNKS = len(chunks)
    UPPER_APART = len(upper_apart)
    ALL_APART = UPPER_APART + len(lower_apart)
    ALL_SQUARES = ALL_APART + len(squares)
    FIRST_QUARTER = 4
    beside = {FIRST_QUARTER + 2 * v: v for v in range(CHUNKS)}
    assert max(beside) + 1 + GRAM_BANKS < GROUP_BLOCKS * QUARTERS
    LOTS = len(upper_lots)
    lot_beside = {FIRST_QUARTER + 2 * UPPER_APART + 1 + 2 * n: n for n in range(LOTS)}
    BLOCK_BATCHES, HALF_BLOCKS = 2 * BLOCK_PAIRS, GROUP_BLOCKS // 2
    assert BLOCK_BATCHES == QUAD and HALF_BLOCKS == QUADS
    half_chunks = ([("apart", range(QUAD, F - 1)), ("apart", range(0, QUAD - 1))]
                   + [("squares", c) for c in squares])
    HALF_CHUNKS, HALF_APART = len(half_chunks), 2
    POOL_LOTS = (len(lower_lots), 2)
    HALF_QUARTERS = HALF_BLOCKS * QUARTERS
    last_beside = {v * 5 // 3: v for v in range(CHUNKS + HALF_CHUNKS)}
    last_lot_beside = {5 + 2 * n: n for n in range(LOTS)}
    last_lot_beside.update({GROUP_BLOCKS * QUARTERS - 1 - 2 * (LOTS - n): LOTS + n - 1 for n in range(1, LOTS + 1)})
    assert min(q for q, v in last_beside.items() if v >= CHUNKS) >= HALF_QUARTERS
    parts = [(QUAD, F - 1), (QUAD // 2, QUAD), (0, QUAD // 2)]
    PARTS = len(parts)
    last_parts = [(0, (QUAD, F - 1), 0), (0, (0, QUAD), 4), (1, (QUAD, F - 1), 0), (1, (0, 2 * STEP), 2),
                  (1, (2 * STEP, 3 * STEP), 3), (1, (3 * STEP, QUAD), 4)]
    assert len(squares) == len(lower_lots) == 4
    lots_block = max(lot_beside) // QUARTERS
    chunks_block = max(beside) // QUARTERS
    assert lots_block < chunks_block

    x_blocks = x.rearrange("(k b) f d -> k (b f) d", k=BLOCKS).rearrange(
        "k (p j) d -> k p (j d)", j=ROWS_PER_PART)
    out_groups = out.rearrange("(g p two) t -> g p two t", g=GROUPS, two=2)
    out_halves = out.rearrange("(h p) t -> h p t", p=P)[2 * (GROUPS - 1):]

    ctx = ExitStack()
    with ctx:
        def sb(name, shape):
            return ctx.enter_context(nc.sbuf_tensor(name, shape, fp32))

        def sem(name):
            return ctx.enter_context(nc.semaphore(name))

        x_rows = sb("x_rows", [P, X_SLOTS, ROWS_PER_PART * D])
        x_flipped = sb("x_flipped", [P, FLIP_SLOTS, BLOCK_ROWS])
        lower = sb("lower", [P, 2, QUAD - 1, 2, QUAD])
        upper = sb("upper", [P, 2, F - 1, 2, QUAD])
        triangles = [sb(f"triangles{i}", [P, 2, TRI]) for i in range(2)]
        apart = [sb("lower_apart", [P, 2, QUAD - 1, 2, QUAD]), sb("upper_apart", [P, 2, QUAD - 1, 2, QUAD])]
        ident = sb("ident", [P, P])
        flip_ps = [ctx.enter_context(nc.psum_tensor(f"flip_ps{i}", [P, BANK], fp32)) for i in range(FLIP_BANKS)]
        gram_ps = [ctx.enter_context(nc.psum_tensor(f"gram_ps{i}", [P, BANK], fp32)) for i in range(GRAM_BANKS)]
        zeroed = sem("zeroed")
        ident_ready = sem("ident_ready")
        x_loaded = [sem(f"x_loaded{i}") for i in range(X_SLOTS)]
        first_loaded = [sem(f"first_loaded{q}") for q in range(PIECED * QUARTERS)]
        flip_in_psum = sem("flip_in_psum")
        flip_in_sbuf = sem("flip_in_sbuf")
        gram_in_psum = sem("gram_in_psum")
        even_in_sbuf = sem("even_in_sbuf")
        odd_in_sbuf = sem("odd_in_sbuf")
        tri_in_sbuf = sem("tri_in_sbuf")
        lots_in_sbuf = sem("lots_in_sbuf")
        stored = [sem(f"stored{h}") for h in range(PARTS)]
        last_in_sbuf = sem("last_in_sbuf")
        low_lots_in_sbuf = sem("low_lots_in_sbuf")
        last_stored = sem("last_stored")
        block = ctx.enter_context(nc.Block())

        def over_groups(engine, body):
            body(0, 0)
            with engine.Fori(0, (GROUPS - 2) // 2) as i:
                body(i * 2 + 1, 1)
                body(i * 2 + 2, 0)
            body(GROUPS - 1, 1)

        def gram_parts(g, parity, u, q):
            products = gram_ps[q % GRAM_BANKS][:, :].rearrange("r (n c) -> r n c", c=P)
            for two in range(2):
                if last(g):
                    quad, to_two = u % HALF_BLOCKS, u // HALF_BLOCKS
                    a = q * PER_BANK * 2 + two
                    at = slice(a, a + PER_BANK * 2 - 1, 2)
                else:
                    quad, to_two = u // QUAD_BLOCKS, two
                    a = u % QUAD_BLOCKS * BLOCK_PAIRS + q * PER_BANK
                    at = slice(a, a + PER_BANK)
                for half, rows in enumerate((lower, upper)):
                    r, columns = two * F + half * QUAD, rows.shape[2]
                    yield (rows[quad * QUAD:(quad + 1) * QUAD, parity, :, to_two, at].rearrange("r c n -> r n c"),
                           products[r:r + QUAD, :, two * F:two * F + columns])

        def below_diagonal(parity, c, twos=slice(0, 2)):
            half, first_column = c // QUAD, c // QUAD * QUAD
            rows = QUAD - 1 - (c - first_column)
            return (triangles[parity][:, twos, row_start[c]:row_start[c] + rows],
                    apart[half][:, parity, c - first_column, twos, QUAD - rows:QUAD])

        def very_last(g, u, q):
            return last(g) and u == GROUP_BLOCKS - 1 and q == QUARTERS - 1

        def first(g):
            return isinstance(g, int) and g == 0

        def last(g):
            return isinstance(g, int) and g == GROUPS - 1

        @block.gpsimd
        def _(pool):
            pool.memset(ident[:, :], 0.0).then_inc(zeroed, 1)
            pool.wait_ge(zeroed, 1)
            pool.affine_select(out=ident[:, :], in_=ident[:, :], compare_op=ALU.not_equal, fill=1.0,
                               base=0, pattern=[[-1, P]], channel_multiplier=1).then_inc(ident_ready, 1)
            for h in range(2):
                pool.wait_ge(tri_in_sbuf, (GROUPS - 1) * CHUNKS + h * HALF_CHUNKS + HALF_APART)
                for columns in lower_lots[:POOL_LOTS[h]]:
                    for c in columns:
                        t = pool.tensor_copy(*below_diagonal(1, c, slice(h, h + 1)))
                    t.then_inc(low_lots_in_sbuf, 1)

        @block.sync
        def _(sp):
            for k in range(PIECED):
                for q in range(QUARTERS):
                    part = slice(q * PER_BANK * D, (q + 1) * PER_BANK * D)
                    sp.dma_start(x_rows[:, k, part], x_blocks[k][:, part])\
                      .then_inc(first_loaded[k * QUARTERS + q], 16)
            for k in range(PIECED, X_SLOTS):
                sp.dma_start(x_rows[:, k, :], x_blocks[k]).then_inc(x_loaded[k], 16)

            def store(g, parity, rows, done):
                a, b = row_start[rows[0]], row_start[rows[1]]
                sp.dma_start(out_groups[g][:, :, a:b], triangles[parity][:, :, a:b]).then_inc(done, 16)

            def body(g, parity):
                for u in range(GROUP_BLOCKS):
                    if not (last(g) and u + X_SLOTS >= GROUP_BLOCKS):
                        sp.wait_ge(flip_in_psum, (g * GROUP_BLOCKS + u + 1) * QUARTERS)
                        sp.dma_start(x_rows[:, u % X_SLOTS, :], x_blocks[g * GROUP_BLOCKS + (u + X_SLOTS)])\
                          .then_inc(x_loaded[u % X_SLOTS], 16)
                    if u == lots_block and not first(g):
                        sp.wait_ge(lots_in_sbuf, g * LOTS)
                        store(g - 1, 1 - parity, parts[0], stored[0])
                    if u == chunks_block and not first(g):
                        sp.wait_ge(tri_in_sbuf, g * CHUNKS)
                        for h in range(1, PARTS):
                            store(g - 1, 1 - parity, parts[h], stored[h])

            over_groups(sp, body)

            def store_half(h, rows, run):
                if run:
                    sp.wait_ge(tri_in_sbuf, (GROUPS - 1) * CHUNKS + h * HALF_CHUNKS + HALF_APART + run)
                    sp.wait_ge(low_lots_in_sbuf, h * POOL_LOTS[0] + min(run, POOL_LOTS[h]))
                    if run > POOL_LOTS[h]:
                        sp.wait_ge(lots_in_sbuf, (GROUPS + h) * LOTS + (run - POOL_LOTS[h]))
                else:
                    sp.wait_ge(lots_in_sbuf, (GROUPS + h) * LOTS)
                a, b = row_start[rows[0]], row_start[rows[1]]
                sp.dma_start(out_halves[h][:, a:b], triangles[1][:, h, a:b]).then_inc(last_stored, 16)

            for h, rows, run in last_parts:
                store_half(h, rows, run)
            for h in range(PARTS):
                sp.wait_ge(stored[h], 16 * (GROUPS - 1))
            sp.wait_ge(last_stored, 16 * len(last_parts))

        @block.tensor
        def _(pe):
            def flip(g, u, q):
                if first(g) and u < PIECED:
                    pe.wait_ge(first_loaded[u * QUARTERS + q], 16)
                elif q == 0:
                    pe.wait_ge(x_loaded[u % X_SLOTS],
                               (g * (GROUP_BLOCKS // X_SLOTS) + (u // X_SLOTS + (u % X_SLOTS >= PIECED))) * 16)
                if not (first(g) and u * QUARTERS + q < FLIP_BANKS):
                    pe.wait_ge(flip_in_sbuf, g * GROUP_BLOCKS * QUARTERS + (u * QUARTERS + q + 1 - FLIP_BANKS))
                for n in range(PER_BANK):
                    j = q * PER_BANK + n
                    t = pe.transpose(flip_ps[q % FLIP_BANKS][:, n * P:(n + 1) * P],
                                     x_rows[:, u % X_SLOTS, j * D:(j + 1) * D], ident[:, :])
                t.then_inc(flip_in_psum, 1)

            def by_batch(pair):
                return pair.rearrange("p (two f) -> p two f", two=2)[:, :, :F - 1]

            def gram(g, u, q):
                if q == 0:
                    pe.wait_ge(flip_in_sbuf, (g * GROUP_BLOCKS + (u + 1)) * QUARTERS)
                if not (first(g) and u * QUARTERS + q < GRAM_BANKS):
                    pe.wait_ge(odd_in_sbuf if q % 2 else even_in_sbuf,
                               g * (GROUP_BLOCKS * QUARTERS // 2) + (u * QUARTERS + q + 2 - GRAM_BANKS) // 2)
                for n in range(PER_BANK):
                    t = (q * PER_BANK + n) * P
                    pair = x_flipped[:, u % FLIP_SLOTS, t:t + P]
                    m = pe.matmul(by_batch(gram_ps[q % GRAM_BANKS][:, n * P:(n + 1) * P]), pair, by_batch(pair),
                                  start=True, stop=True)
                m.then_inc(gram_in_psum, 1)

            def body(g, parity):
                for u in range(GROUP_BLOCKS):
                    ahead = 1 if first(g) and u == 0 else 0
                    for q in range(ahead):
                        flip(g, u + 1, q)
                    for q in range(QUARTERS):
                        if q + ahead < QUARTERS and not (last(g) and u == GROUP_BLOCKS - 1):
                            flip(g, u + 1, q + ahead)
                        gram(g, u, q)

            pe.wait_ge(ident_ready, 1)
            for q in range(QUARTERS):
                flip(0, 0, q)
            over_groups(pe, body)

        @block.scalar
        def _(act):
            def flip_out(g, u, q):
                act.wait_ge(flip_in_psum, g * GROUP_BLOCKS * QUARTERS + (u * QUARTERS + q + 1))
                rows = x_flipped[:, u % FLIP_SLOTS, :].rearrange("d (p j) -> d j p", j=ROWS_PER_PART)
                act.activation(rows[:, q * PER_BANK:(q + 1) * PER_BANK, :],
                               flip_ps[q % FLIP_BANKS][:, :].rearrange("d (j p) -> d j p", p=P), ACT.Copy)\
                   .then_inc(flip_in_sbuf, 1)

            def copy_lot(parity, n):
                for c in upper_lots[n]:
                    a = act.activation(*below_diagonal(parity, c), ACT.Copy)
                a.then_inc(lots_in_sbuf, 1)

            def copy_half_lot(h, n):
                if n in (0, LOTS):
                    act.wait_ge(tri_in_sbuf, (GROUPS - 1) * CHUNKS + h * HALF_CHUNKS + (2 if n else 1))
                for c in (upper_lots + lower_lots[POOL_LOTS[h]:])[n]:
                    a = act.activation(*below_diagonal(1, c, slice(h, h + 1)), ACT.Copy)
                a.then_inc(lots_in_sbuf, 1)

            def body(g, parity):
                for u in range(GROUP_BLOCKS):
                    for q in range(QUARTERS):
                        if not (last(g) and u == GROUP_BLOCKS - 1):
                            flip_out(g, u + 1, q)
                        if q % 2 == 0:
                            act.wait_ge(gram_in_psum, g * GROUP_BLOCKS * QUARTERS + (u * QUARTERS + q + 1))
                            for to, products in gram_parts(g, parity, u, q):
                                a = act.activation(to, products, ACT.Copy)
                            a.then_inc(even_in_sbuf, 1)
                        if very_last(g, u, q):
                            act.wait_ge(gram_in_psum, GROUPS * GROUP_BLOCKS * QUARTERS)
                            for to, products in list(gram_parts(g, parity, u, q))[:2]:
                                a = act.activation(to, products, ACT.Copy)
                            a.then_inc(last_in_sbuf, 1)
                        n = (last_lot_beside if last(g) else lot_beside).get(u * QUARTERS + q)
                        if n is not None and n >= LOTS:
                            copy_half_lot(0, n - LOTS)
                        elif n is not None and not first(g):
                            if n == 0:
                                act.wait_ge(tri_in_sbuf, (g - 1) * CHUNKS + UPPER_APART)
                            copy_lot(1 - parity, n)

            for q in range(QUARTERS):
                flip_out(0, 0, q)
            over_groups(act, body)
            for n in range(LOTS + len(lower_lots) - POOL_LOTS[1]):
                copy_half_lot(1, n)

        @block.vector
        def _(dve):
            def triangle(g, parity, v):
                if v == 0:
                    dve.wait_ge(even_in_sbuf, (g + 1) * (GROUP_BLOCKS * QUARTERS // 2))
                    dve.wait_ge(odd_in_sbuf, (g + 1) * (GROUP_BLOCKS * QUARTERS // 2))
                    if parity == 1:
                        for h in range(PARTS):
                            dve.wait_ge(stored[h], g * 16)
                kind, columns = chunks[v]
                if kind == "apart":
                    half, a, n = columns[0] // QUAD, columns[0] % QUAD, len(columns)
                    t = dve.transpose(apart[half][:, parity, a:a + n],
                                      (lower, upper)[half][:, parity, columns[0]:columns[0] + n])
                elif kind == "squares":
                    for c in columns:
                        at = row_start[c] + QUAD - (c + 1)
                        t = dve.transpose(triangles[parity][:, :, at:at + QUAD], upper[:, parity, c])
                else:
                    if v == ALL_SQUARES:
                        dve.wait_ge(tri_in_sbuf, g * CHUNKS + ALL_APART)
                    for c in columns:
                        t = dve.tensor_copy(*below_diagonal(parity, c))
                t.then_inc(tri_in_sbuf, 1)

            def half_triangle(h, v):
                if v == 0:
                    banks = ((GROUPS - 1) * GROUP_BLOCKS + (h + 1) * HALF_BLOCKS) * QUARTERS // 2
                    dve.wait_ge(even_in_sbuf, banks)
                    dve.wait_ge(odd_in_sbuf, banks)
                    if h == 1:
                        dve.wait_ge(last_in_sbuf, 1)
                    if h == 0:
                        for part in range(PARTS):
                            dve.wait_ge(stored[part], (GROUPS - 2) * 16)
                kind, columns = half_chunks[v]
                if kind == "apart":
                    half, a, n = columns[0] // QUAD, columns[0] % QUAD, len(columns)
                    t = dve.transpose(apart[half][:, 1, a:a + n, h],
                                      (lower, upper)[half][:, 1, columns[0]:columns[0] + n, h])
                else:
                    for c in columns:
                        at = row_start[c] + QUAD - (c + 1)
                        t = dve.transpose(triangles[1][:, h, at:at + QUAD], upper[:, 1, c, h])
                t.then_inc(tri_in_sbuf, 1)

            def body(g, parity):
                for u in range(GROUP_BLOCKS):
                    for q in range(QUARTERS):
                        if q % 2:
                            dve.wait_ge(gram_in_psum, g * GROUP_BLOCKS * QUARTERS + (u * QUARTERS + q + 1))
                            for to, products in list(gram_parts(g, parity, u, q))[2 if very_last(g, u, q) else 0:]:
                                t = dve.tensor_copy(to, products)
                            t.then_inc(odd_in_sbuf, 1)
                        v = (last_beside if last(g) else beside).get(u * QUARTERS + q)
                        if v is not None and v >= CHUNKS:
                            half_triangle(0, v - CHUNKS)
                        elif v is not None and not first(g):
                            triangle(g - 1, 1 - parity, v)

            over_groups(dve, body)
            for v in range(HALF_CHUNKS):
                half_triangle(1, v)


def kernel(r_dense_features):
    import numpy as np
    import concourse.bacc as bacc
    from concourse.bass_utils import run_bass_kernel_spmd

    x = np.ascontiguousarray(r_dense_features)
    b, f, _ = x.shape
    nc = bacc.Bacc("TRN2", target_bir_lowering=False, num_devices=1)
    x_dram = nc.dram_tensor("x_dram", x.shape, mybir.dt.float32, kind="ExternalInput").ap()
    out_dram = nc.dram_tensor("out_dram", (b, f * (f - 1) // 2), mybir.dt.float32, kind="ExternalOutput").ap()
    build_gram_triangle(nc, x_dram, out_dram)
    r = run_bass_kernel_spmd(nc, [{"x_dram": x}], core_ids=[0])
    return r.results[0]["out_dram"]
```
